# Optimizing a Trainium2 kernel written in Bass

```python
import numpy as np
import jax
import jax.numpy as jnp

def _softmax(x, axis=-1):
    return jax.nn.softmax(x, axis=axis)

def _gelu(x):
    return jax.nn.gelu(x, approximate=True)

def _silu(x):
    return jax.nn.silu(x)

def _sigmoid(x):
    return jax.nn.sigmoid(x)

def _layernorm(x, axis=-1, eps=1e-05):
    m = jnp.mean(x, axis=axis, keepdims=True)
    v = jnp.var(x, axis=axis, keepdims=True)
    return (x - m) / jnp.sqrt(v + eps)

def _scatter_add(tgt, idx, src, axis=0):
    return tgt.at[idx].add(src)

def _segment_sum(src, seg, n):
    return jax.ops.segment_sum(src, seg, n)
kernel_name = 'mk_dlrm_tower_d1_rec_r8_63a06d'

def setup_inputs(seed: int=0):
    np.random.seed(seed)
    _w = jnp.asarray

    def _rec_inputs():
        import jax
        import jax.numpy as jnp
        _tk = jax.random.key(seed)
        ids = jnp.stack([jax.random.randint(jax.random.fold_in(_tk, 200 + f), (2048,), 0, v, jnp.int32) for f, v in enumerate([1250, 1250, 1250, 1000, 1250, 1000, 125000, 1250, 1250, 1250, 12500, 12500, 12500, 1250, 12500, 1250, 12500, 1000, 12500, 1000, 1000, 12500, 12500, 1250, 1000, 1000])], axis=1)
        tbl_0 = 0.05 * jax.random.normal(jax.random.fold_in(_tk, 500 + 0), (1250, 128), jnp.float32)
        tbl_1 = 0.05 * jax.random.normal(jax.random.fold_in(_tk, 500 + 1), (1250, 128), jnp.float32)
        tbl_2 = 0.05 * jax.random.normal(jax.random.fold_in(_tk, 500 + 2), (1250, 128), jnp.float32)
        tbl_3 = 0.05 * jax.random.normal(jax.random.fold_in(_tk, 500 + 3), (1000, 128), jnp.float32)
        tbl_4 = 0.05 * jax.random.normal(jax.random.fold_in(_tk, 500 + 4), (1250, 128), jnp.float32)
        tbl_5 = 0.05 * jax.random.normal(jax.random.fold_in(_tk, 500 + 5), (1000, 128), jnp.float32)
        tbl_6 = 0.05 * jax.random.normal(jax.random.fold_in(_tk, 500 + 6), (125000, 128), jnp.float32)
        tbl_7 = 0.05 * jax.random.normal(jax.random.fold_in(_tk, 500 + 7), (1250, 128), jnp.float32)
        tbl_8 = 0.05 * jax.random.normal(jax.random.fold_in(_tk, 500 + 8), (1250, 128), jnp.float32)
        tbl_9 = 0.05 * jax.random.normal(jax.random.fold_in(_tk, 500 + 9), (1250, 128), jnp.float32)
        tbl_10 = 0.05 * jax.random.normal(jax.random.fold_in(_tk, 500 + 10), (12500, 128), jnp.float32)
        tbl_11 = 0.05 * jax.random.normal(jax.random.fold_in(_tk, 500 + 11), (12500, 128), jnp.float32)
        tbl_12 = 0.05 * jax.random.normal(jax.random.fold_in(_tk, 500 + 12), (12500, 128), jnp.float32)
        tbl_13 = 0.05 * jax.random.normal(jax.random.fold_in(_tk, 500 + 13), (1250, 128), jnp.float32)
        tbl_14 = 0.05 * jax.random.normal(jax.random.fold_in(_tk, 500 + 14), (12500, 128), jnp.float32)
        tbl_15 = 0.05 * jax.random.normal(jax.random.fold_in(_tk, 500 + 15), (1250, 128), jnp.float32)
        tbl_16 = 0.05 * jax.random.normal(jax.random.fold_in(_tk, 500 + 16), (12500, 128), jnp.float32)
        tbl_17 = 0.05 * jax.random.normal(jax.random.fold_in(_tk, 500 + 17), (1000, 128), jnp.float32)
        tbl_18 = 0.05 * jax.random.normal(jax.random.fold_in(_tk, 500 + 18), (12500, 128), jnp.float32)
        tbl_19 = 0.05 * jax.random.normal(jax.random.fold_in(_tk, 500 + 19), (1000, 128), jnp.float32)
        tbl_20 = 0.05 * jax.random.normal(jax.random.fold_in(_tk, 500 + 20), (1000, 128), jnp.float32)
        tbl_21 = 0.05 * jax.random.normal(jax.random.fold_in(_tk, 500 + 21), (12500, 128), jnp.float32)
        tbl_22 = 0.05 * jax.random.normal(jax.random.fold_in(_tk, 500 + 22), (12500, 128), jnp.float32)
        tbl_23 = 0.05 * jax.random.normal(jax.random.fold_in(_tk, 500 + 23), (1250, 128), jnp.float32)
        tbl_24 = 0.05 * jax.random.normal(jax.random.fold_in(_tk, 500 + 24), (1000, 128), jnp.float32)
        tbl_25 = 0.05 * jax.random.normal(jax.random.fold_in(_tk, 500 + 25), (1000, 128), jnp.float32)
        _rk = jax.random.fold_in(_tk, 7)
        r_dense_x = -0.000514642 + 1.00011 * jax.random.normal(jax.random.fold_in(_rk, 101), (2048, 128), jnp.float32)
        W_top1 = 0.0456912 * jax.random.normal(jax.random.fold_in(_tk, 801), (479, 512), jnp.float32)
        W_top2 = 0.0441942 * jax.random.normal(jax.random.fold_in(_tk, 802), (512, 256), jnp.float32)
        W_top3 = 0.0625 * jax.random.normal(jax.random.fold_in(_tk, 803), (256, 1), jnp.float32)
        b_top1 = jnp.zeros((512,), jnp.float32)
        b_top2 = jnp.zeros((256,), jnp.float32)
        return (r_dense_x, ids, tbl_0, tbl_1, tbl_2, tbl_3, tbl_4, tbl_5, tbl_6, tbl_7, tbl_8, tbl_9, tbl_10, tbl_11, tbl_12, tbl_13, tbl_14, tbl_15, tbl_16, tbl_17, tbl_18, tbl_19, tbl_20, tbl_21, tbl_22, tbl_23, tbl_24, tbl_25, W_top1, b_top1, W_top2, b_top2, W_top3)
    r_dense_x, ids, tbl_0, tbl_1, tbl_2, tbl_3, tbl_4, tbl_5, tbl_6, tbl_7, tbl_8, tbl_9, tbl_10, tbl_11, tbl_12, tbl_13, tbl_14, tbl_15, tbl_16, tbl_17, tbl_18, tbl_19, tbl_20, tbl_21, tbl_22, tbl_23, tbl_24, tbl_25, W_top1, b_top1, W_top2, b_top2, W_top3 = _rec_inputs()

    def _L0_rec_setup():
        import jax, jax.numpy as jnp
        import numpy as np
        F = 26
        D = 128
        B = 2048
        _TRIU_I, _TRIU_J = np.triu_indices(F + 1, k=1)
        _TRIU_I = jnp.asarray(_TRIU_I)
        _TRIU_J = jnp.asarray(_TRIU_J)
        key = jax.random.key(seed)
        k1, k2 = jax.random.split(key)
        sparse_x = jax.random.normal(k1, (B, F, D), dtype=jnp.float32)
        dense_x = jax.random.normal(k2, (B, D), dtype=jnp.float32)
        return {'sparse_x': sparse_x, 'dense_x': dense_x}
    _L0_rec_all = _L0_rec_setup()
    _L0_rec_in = {k: v for k, v in _L0_rec_all.items() if k in ()}
    del _L0_rec_all
    return {'r_dense_x': r_dense_x, 'ids': ids, 'tbl_0': tbl_0, 'tbl_1': tbl_1, 'tbl_2': tbl_2, 'tbl_3': tbl_3, 'tbl_4': tbl_4, 'tbl_5': tbl_5, 'tbl_6': tbl_6, 'tbl_7': tbl_7, 'tbl_8': tbl_8, 'tbl_9': tbl_9, 'tbl_10': tbl_10, 'tbl_11': tbl_11, 'tbl_12': tbl_12, 'tbl_13': tbl_13, 'tbl_14': tbl_14, 'tbl_15': tbl_15, 'tbl_16': tbl_16, 'tbl_17': tbl_17, 'tbl_18': tbl_18, 'tbl_19': tbl_19, 'tbl_20': tbl_20, 'tbl_21': tbl_21, 'tbl_22': tbl_22, 'tbl_23': tbl_23, 'tbl_24': tbl_24, 'tbl_25': tbl_25, 'W_top1': W_top1, 'b_top1': b_top1, 'W_top2': W_top2, 'b_top2': b_top2, 'W_top3': W_top3}

def reference(r_dense_x, ids, tbl_0, tbl_1, tbl_2, tbl_3, tbl_4, tbl_5, tbl_6, tbl_7, tbl_8, tbl_9, tbl_10, tbl_11, tbl_12, tbl_13, tbl_14, tbl_15, tbl_16, tbl_17, tbl_18, tbl_19, tbl_20, tbl_21, tbl_22, tbl_23, tbl_24, tbl_25, W_top1, b_top1, W_top2, b_top2, W_top3):
    import jax
    import jax.numpy as jnp

    def _L0_rec_ref(sparse_x, dense_x):
        import jax, jax.numpy as jnp
        import numpy as np
        F = 26
        D = 128
        B = 2048
        _TRIU_I, _TRIU_J = np.triu_indices(F + 1, k=1)
        _TRIU_I = jnp.asarray(_TRIU_I)
        _TRIU_J = jnp.asarray(_TRIU_J)
        combined = jnp.concatenate([sparse_x, dense_x[:, None, :]], axis=1)
        interact = jnp.einsum('bfd,bgd->bfg', combined, combined)
        return interact[:, _TRIU_I, _TRIU_J]
    e = jnp.stack([tbl_0[ids[:, 0]], tbl_1[ids[:, 1]], tbl_2[ids[:, 2]], tbl_3[ids[:, 3]], tbl_4[ids[:, 4]], tbl_5[ids[:, 5]], tbl_6[ids[:, 6]], tbl_7[ids[:, 7]], tbl_8[ids[:, 8]], tbl_9[ids[:, 9]], tbl_10[ids[:, 10]], tbl_11[ids[:, 11]], tbl_12[ids[:, 12]], tbl_13[ids[:, 13]], tbl_14[ids[:, 14]], tbl_15[ids[:, 15]], tbl_16[ids[:, 16]], tbl_17[ids[:, 17]], tbl_18[ids[:, 18]], tbl_19[ids[:, 19]], tbl_20[ids[:, 20]], tbl_21[ids[:, 21]], tbl_22[ids[:, 22]], tbl_23[ids[:, 23]], tbl_24[ids[:, 24]], tbl_25[ids[:, 25]]], axis=1)
    z = _L0_rec_ref(e, r_dense_x)
    z = z.reshape(z.shape[0], -1)
    h = jnp.concatenate([z, r_dense_x], axis=1)
    h = jnp.maximum(h @ W_top1 + b_top1, 0.0)
    h = jnp.maximum(h @ W_top2 + b_top2, 0.0)
    y = h @ W_top3
    return y

_drawn_inputs = setup_inputs


def setup_inputs(seed=0):
    import zlib

    import numpy as np

    out = dict(_drawn_inputs(seed))
    spreads = {'b_top1': (0.0, 0.1), 'b_top2': (0.0, 0.1)}
    factors = {}
    for name, (base, spread) in spreads.items():
        noise = np.random.default_rng([zlib.crc32(name.encode()), seed]).standard_normal(out[name].shape)
        drawn = base * np.exp(spread * noise) if base else spread * noise
        out[name] = jnp.asarray(drawn.astype(out[name].dtype))
    for name, factor in factors.items():
        out[name] = (out[name] * factor).astype(out[name].dtype)
    return out
```

```python
from contextlib import ExitStack

import concourse.bass as bass
from concourse import mybir
from concourse.alu_op_type import AluOpType as ALU

F32 = mybir.dt.float32
I32 = mybir.dt.int32
ACT = mybir.ActivationFunctionType

P = 128
TILES = 4
CREDIT = 1
SLOTS = 32
QUAD = 4
BANK = 512


def build(nc, dense_t, ids, tables, w1, b1, w2, b2, w3, out):
    nf = len(tables)
    feats = nf + 1
    batch = dense_t.shape[1]
    n_super = TILES * P
    supers = batch // n_super
    groups = P // QUAD
    groups_super = n_super // QUAD
    assert groups_super == P and batch % n_super == 0
    pairs = feats * (feats - 1) // 2
    kz = 117
    n_kz = pairs // kz
    assert kz * n_kz == pairs
    d1, d2 = w1.shape[1], w2.shape[1]
    m1, m2 = d1 // P, d2 // P

    turn_groups = [list(range(f, min(f + 4, nf))) for f in range(0, nf, 4)]
    n_turn = len(turn_groups)
    assert (n_turn * TILES) % 2 == 0
    per_bank = BANK // (QUAD * feats)
    per_fill = 2 * per_bank
    n_gram = groups // per_fill
    assert n_gram * per_fill == groups and n_gram % 2 == 0
    pair_start = [q * feats - q * (q + 1) // 2 for q in range(feats)]
    col_groups = [list(range(q, min(q + 4, feats - 1))) for q in range(0, feats - 1, 4)]
    n_cols = len(col_groups)
    tail = ([("cols", g) for g in range(n_cols)] + [("zt", k) for k in range(n_kz)]
            + [("h1", m) for m in range(m1)] + [("h2", m) for m in range(m2)] + [("y", 0)])
    tail_bank = {key: j % 2 for j, key in enumerate(tail)}
    tail_nth = {key: j // 2 for j, key in enumerate(tail)}
    tail_per = [len([j for j in range(len(tail)) if j % 2 == b]) for b in range(2)]

    with ExitStack() as ctx:
        def sb(name, shape, dt=F32):
            return ctx.enter_context(nc.sbuf_tensor(name, shape, dt))

        def psum(name, shape):
            return ctx.enter_context(nc.psum_tensor(name, shape, F32))

        def sem(name):
            return ctx.enter_context(nc.semaphore(name))

        ident = sb("ident", [P, P])
        ids_sb = [sb(f"ids_sb{k}", [P, nf], I32) for k in range(TILES)]
        raw = [sb(f"raw{k}", [P, nf, P]) for k in range(TILES)]
        xt = [sb(f"xt{k}", [P, P, SLOTS]) for k in range(TILES)]
        dense_sb = sb("dense_sb", [P, batch])
        gram = sb("gram", [P, groups_super, feats])
        z = sb("z", [P, QUAD, pairs])
        zt = sb("zt", [P, n_kz, n_super])
        h1 = sb("h1", [P, m1, n_super])
        h2 = sb("h2", [P, m2, n_super])
        y = sb("y", [1, batch])
        w1z_sb = sb("w1z_sb", [P, n_kz, d1])
        w1d_sb = sb("w1d_sb", [P, d1])
        w2_sb = sb("w2_sb", [P, m1, d2])
        w3_sb = sb("w3_sb", [P, m2])
        b1_sb = sb("b1_sb", [P, m1])
        b2_sb = sb("b2_sb", [P, m2])

        turn_ps = [psum(f"turn_ps{b}", [P, BANK]) for b in range(2)]
        gram_ps = [psum(f"gram_ps{b}", [P, 2, BANK]) for b in range(2)]
        tail_ps = [psum(f"tail_ps{b}", [P, BANK]) for b in range(2)]

        ident_ready = sem("ident_ready")
        dense_in = sem("dense_in")
        slots_opened = sem("slots_opened")
        ids_opened = sem("ids_opened")
        ids_in = [sem(f"ids_in{k}") for k in range(TILES)]
        rows_in = [[sem(f"rows_in{k}_{g}") for g in range(n_turn)] for k in range(TILES)]
        weights_in = sem("weights_in")
        ident_zero = sem("ident_zero")
        pad_ready = sem("pad_ready")
        turn_full = [sem(f"turn_full{k}") for k in range(TILES)]
        turn_copied = [sem(f"turn_copied{b}") for b in range(2)]
        dense_copied = sem("dense_copied")
        gram_full = sem("gram_full")
        gram_act = [sem(f"gram_act{b}") for b in range(2)]
        gram_dve = [sem(f"gram_dve{b}") for b in range(2)]
        tail_full = {kind: sem(f"{kind}_full") for kind in ("cols", "zt", "h1", "h2", "y")}
        tail_copied = [sem(f"tail_copied{b}") for b in range(2)]
        y_stored = sem("y_stored")

        block = ctx.enter_context(nc.Block())

        def turn_copy(eng, copy, T, k, g):
            n = n_turn * k + g
            fs = turn_groups[g]
            eng.wait_ge(turn_full[k], T * n_turn + (g + 1 + CREDIT))
            src = turn_ps[n % 2][:, 0:len(fs) * P].rearrange("p (f b) -> p b f", b=P)
            copy(xt[k][:, :, fs[0]:fs[-1] + 1], src).then_inc(turn_copied[n % 2], 1)

        def gram_copy(eng, copy, done, quads, T, k, n):
            m = n_gram * k + n
            eng.wait_ge(gram_full, T * (n_gram * TILES) + (m + 1))
            if m == 0:
                eng.wait_ge(tail_full["cols"], T * n_cols + CREDIT)
            g0 = groups * k + per_fill * n
            for s in quads:
                rows = slice(32 * s, 32 * s + 32)
                src = gram_ps[m % 2][rows, :, 0:per_bank * QUAD * feats].rearrange(
                    "p b (g c) -> p b g c", g=per_bank)[:, :, :, s * feats:(s + 1) * feats]
                dst = gram[rows, g0:g0 + per_fill, :].rearrange("p (b g) c -> p b g c", b=2)
                last = copy(dst, src)
            last.then_inc(done[m % 2], 1)

        def tail_wait(eng, key, T):
            kind, j = key
            eng.wait_ge(tail_full[kind], T * len([1 for other in tail if other[0] == kind]) + (j + 1 + CREDIT))

        def tail_copies(eng, copy, bias_relu, bank, T):
            for key in tail:
                if tail_bank[key] != bank:
                    continue
                kind, j = key
                tail_wait(eng, key, T)
                ps = tail_ps[bank]
                if kind == "cols":
                    for c, q in enumerate(col_groups[j]):
                        n = feats - 1 - q
                        src = ps[:, c * P:(c + 1) * P].rearrange("g (s p) -> g s p", s=QUAD)[:, :, q + 1:feats]
                        last = copy(z[:, :, pair_start[q]:pair_start[q] + n], src)
                elif kind == "zt":
                    src = ps[0:kz, :].rearrange("p (s g) -> p g s", s=QUAD)
                    last = copy(zt[0:kz, j, :].rearrange("p (g s) -> p g s", s=QUAD), src)
                elif kind == "h1":
                    last = bias_relu(h1[:, j, :], ps[:, :], b1_sb[:, j:j + 1])
                elif kind == "h2":
                    last = bias_relu(h2[:, j, :], ps[:, :], b2_sb[:, j:j + 1])
                else:
                    last = copy(y[:, bass.ds(T * n_super, n_super)], ps[0:1, :])
                last.then_inc(tail_copied[bank], 1)

        @block.sync
        def _(sp):
            def load_ids(k, T):
                sp.wait_ge(turn_full[k], T * n_turn + CREDIT)
                sp.sem_inc(ids_opened, 1)
                sp.dma_start(ids_sb[k][:, :], ids[:, bass.ds(T * TILES + k, 1), :].rearrange(
                    "p o f -> p (o f)")).then_inc(ids_in[k], 16)

            for k in range(TILES):
                sp.dma_start(ids_sb[k][:, :], ids[:, k, :]).then_inc(ids_in[k], 16)
            sp.dma_start(dense_sb[:, :], dense_t).then_inc(dense_in, 16)
            sp.dma_start(w1z_sb[0:kz, :, :], w1[0:pairs, :].rearrange("(k p) n -> p k n", p=kz)).then_inc(weights_in, 16)
            sp.dma_start(w1d_sb[:, :], w1[pairs:pairs + P, :]).then_inc(weights_in, 16)
            sp.dma_start(w2_sb[:, :, :], w2.rearrange("(k p) n -> p k n", p=P)).then_inc(weights_in, 16)
            sp.dma_start(w3_sb[:, :], w3).then_inc(weights_in, 16)
            sp.dma_start(b1_sb[:, :], b1).then_inc(weights_in, 16)
            sp.dma_start(b2_sb[:, :], b2).then_inc(weights_in, 16)
            with sp.Fori(1, supers) as T:
                for k in range(TILES):
                    load_ids(k, T)

        @block.gpsimd
        def _(pool):
            nc.gpsimd.memset(ident[:, :], 0.0).then_inc(ident_zero, 1)
            pool.wait_ge(ident_zero, 1)
            nc.gpsimd.affine_select(out=ident[:, :], in_=ident[:, :], compare_op=ALU.not_equal, fill=1.0, base=0,
                                    pattern=[[-1, P]], channel_multiplier=1).then_inc(ident_ready, 1)
            with pool.Fori(0, supers) as T:
                for k in range(TILES):
                    pool.wait_ge(ids_in[k], (T + 1) * 16)
                    pool.wait_ge(turn_full[k], T * n_turn + CREDIT)
                    pool.sem_inc(slots_opened, 1)
                    for g, fs in enumerate(turn_groups):
                        for f in fs:
                            nc.gpsimd.indirect_dma_start(
                                out=raw[k][:, f, :], out_offset=None, in_=tables[f],
                                in_offset=bass.IndirectOffsetOnAxis(ap=ids_sb[k][:, f:f + 1], axis=0),
                            ).then_inc(rows_in[k][g], 16)

        @block.tensor
        def _(pe):
            def turn_rows(T, k, g):
                n = n_turn * k + g
                pe.wait_ge(rows_in[k][g], (T + 1) * (16 * len(turn_groups[g])))
                pe.wait_ge(turn_copied[n % 2], T * (n_turn * TILES // 2) + (n // 2 + CREDIT))
                for c, f in enumerate(turn_groups[g]):
                    last = nc.tensor.transpose(turn_ps[n % 2][:, c * P:(c + 1) * P], raw[k][:, f, :], ident[:, :])
                last.then_inc(turn_full[k], 1)

            def products(T, k, n):
                m = n_gram * k + n
                for done in (gram_act, gram_dve):
                    pe.wait_ge(done[m % 2], T * (n_gram * TILES // 2) + (m // 2 + CREDIT))
                for g in range(per_fill):
                    b = (per_fill * n + g) * QUAD
                    col = (g % per_bank) * QUAD * feats
                    last = nc.tensor.matmul(gram_ps[m % 2][:, g // per_bank, col:col + QUAD * feats], 
                                            xt[k][:, b:b + QUAD, :].rearrange("p b f -> p (b f)"),
                                            xt[k][:, b:b + QUAD, 0:feats], start=True, stop=True)
                last.then_inc(gram_full, 1)

            def tail_free(key, T):
                b = tail_bank[key]
                pe.wait_ge(tail_copied[b], T * tail_per[b] + (tail_nth[key] + CREDIT))

            def tail_has(kind, T):
                for b in range(2):
                    nth = [tail_nth[key] for key in tail if key[0] == kind and tail_bank[key] == b]
                    if nth:
                        pe.wait_ge(tail_copied[b], T * tail_per[b] + (max(nth) + 1 + CREDIT))

            def mlp(T):
                for key in tail:
                    kind, j = key
                    ps = tail_ps[tail_bank[key]]
                    if j == 0:
                        if kind == "cols":
                            for b in range(2):
                                for done in (gram_act, gram_dve):
                                    pe.wait_ge(done[b], T * (n_gram * TILES // 2) + (n_gram * TILES // 2 + CREDIT))
                        elif kind == "zt":
                            tail_has("cols", T)
                        elif kind == "h1":
                            tail_has("zt", T)
                            pe.wait_ge(weights_in, 6 * 16)
                            pe.wait_ge(dense_in, 16)
                        elif kind == "h2":
                            tail_has("h1", T)
                        else:
                            tail_has("h2", T)
                    tail_free(key, T)
                    if kind == "cols":
                        for c, q in enumerate(col_groups[j]):
                            last = nc.tensor.transpose(ps[:, c * P:(c + 1) * P], gram[:, :, q], ident[:, :])
                    elif kind == "zt":
                        for s in range(QUAD):
                            last = nc.tensor.transpose(ps[0:kz, s * P:(s + 1) * P], z[:, s, j * kz:(j + 1) * kz],
                                                       ident[:, :])
                    elif kind == "h1":
                        w = slice(j * P, (j + 1) * P)
                        nc.tensor.matmul(ps[:, :], w1d_sb[:, w], dense_sb[:, bass.ds(T * n_super, n_super)],
                                         start=True, stop=False)
                        for c in range(n_kz):
                            last = nc.tensor.matmul(ps[:, :], w1z_sb[0:kz, c, w], zt[0:kz, c, :],
                                                    start=False, stop=(c == n_kz - 1))
                    elif kind == "h2":
                        for c in range(m1):
                            last = nc.tensor.matmul(ps[:, :], w2_sb[:, c, j * P:(j + 1) * P], h1[:, c, :],
                                                    start=(c == 0), stop=(c == m1 - 1))
                    else:
                        for c in range(m2):
                            last = nc.tensor.matmul(ps[0:1, :], w3_sb[:, c:c + 1], h2[:, c, :],
                                                    start=(c == 0), stop=(c == m2 - 1))
                    last.then_inc(tail_full[kind], 1)

            for full in turn_full + list(tail_full.values()):
                pe.sem_inc(full, CREDIT)
            pe.wait_ge(ident_ready, 1)
            with pe.Fori(0, supers) as T:
                for k in range(TILES):
                    for g in range(n_turn):
                        turn_rows(T, k, g)
                    done = n_turn * (k + 1)
                    pe.wait_ge(turn_copied[0], T * (n_turn * TILES // 2) + ((done + 1) // 2 + CREDIT))
                    pe.wait_ge(turn_copied[1], T * (n_turn * TILES // 2) + (done // 2 + CREDIT))
                    pe.wait_ge(dense_copied, T * TILES + (k + 1))
                    pe.wait_ge(pad_ready, 1)
                    for n in range(n_gram):
                        products(T, k, n)
                mlp(T)

        def copies(eng, copy, T, k, bank):
            for g in range(n_turn):
                if (n_turn * k + g) % 2 == bank:
                    turn_copy(eng, copy, T, k, g)

        @block.scalar
        def _(act):
            copy = nc.scalar.copy
            for done in (turn_copied[0], gram_act[0], gram_act[1], tail_copied[0]):
                act.sem_inc(done, CREDIT)
            act.wait_ge(dense_in, 16)
            act.wait_ge(weights_in, 6 * 16)
            with act.Fori(0, supers) as T:
                for k in range(TILES):
                    copies(act, copy, T, k, 0)
                    copy(xt[k][:, :, nf], dense_sb[:, bass.ds(T * n_super + k * P, P)]).then_inc(dense_copied, 1)
                    for n in range(n_gram):
                        gram_copy(act, copy, gram_act, (0, 1), T, k, n)
                tail_copies(act, copy, lambda o, i, b: nc.scalar.activation(o, i, ACT.Relu, bias=b), 0, T)
            act.wait_ge(tail_copied[0], supers * tail_per[0] + CREDIT)
            act.dma_start(out, y[:, :]).then_inc(y_stored, 16)
            act.wait_ge(y_stored, 16)

        @block.vector
        def _(dve):
            copy = nc.vector.tensor_copy
            for k in range(TILES):
                last = nc.vector.memset(xt[k][:, :, feats:], 0.0)
            last.then_inc(pad_ready, 1)
            for done in (turn_copied[1], gram_dve[0], gram_dve[1], tail_copied[1]):
                dve.sem_inc(done, CREDIT)
            dve.wait_ge(weights_in, 6 * 16)
            with dve.Fori(0, supers) as T:
                for k in range(TILES):
                    copies(dve, copy, T, k, 1)
                    for n in range(n_gram):
                        gram_copy(dve, copy, gram_dve, (2, 3), T, k, n)
                tail_copies(dve, copy, lambda o, i, b: nc.vector.tensor_scalar(o, i, b, 0.0, ALU.add, ALU.max), 1, T)


def kernel(**inputs):
    import numpy as np
    import concourse.bacc as bacc
    from concourse.bass_utils import run_bass_kernel_spmd

    nf = inputs["ids"].shape[1]
    batch = inputs["ids"].shape[0]
    arrays = {
        "dense_t": inputs["r_dense_x"].T,
        "ids": np.asarray(inputs["ids"]).reshape(batch // P, P, nf).transpose(1, 0, 2),
        "w1": inputs["W_top1"],
        "b1": np.asarray(inputs["b_top1"]).reshape(-1, P).T,
        "w2": inputs["W_top2"],
        "b2": np.asarray(inputs["b_top2"]).reshape(-1, P).T,
        "w3": np.asarray(inputs["W_top3"]).reshape(-1, P).T,
    }
    for f in range(nf):
        arrays[f"tbl_{f}"] = inputs[f"tbl_{f}"]
    arrays = {n: np.ascontiguousarray(a) for n, a in arrays.items()}
    nc = bacc.Bacc("TRN2", target_bir_lowering=False, num_devices=1)
    ap = {n: nc.dram_tensor(f"in_{n}", a.shape, mybir.dt.from_np(a.dtype), kind="ExternalInput").ap()
          for n, a in arrays.items()}
    y = nc.dram_tensor("y_out", (1, batch), F32, kind="ExternalOutput").ap()
    build(nc, ap["dense_t"], ap["ids"], [ap[f"tbl_{f}"] for f in range(nf)], ap["w1"], ap["b1"], ap["w2"],
          ap["b2"], ap["w3"], y)
    r = run_bass_kernel_spmd(nc, [{f"in_{n}": a for n, a in arrays.items()}], core_ids=[0])
    return r.results[0]["y_out"].reshape(batch, 1)
```

```python
from contextlib import ExitStack

import concourse.bass as bass
from concourse import mybir
from concourse.alu_op_type import AluOpType as ALU

F32 = mybir.dt.float32
F32R = mybir.dt.float32r
I32 = mybir.dt.int32
ACT = mybir.ActivationFunctionType

P = 128
TILES = 4
HALVES = 2
ROWS = 8
RING = 8
LEAD = 7
CREDIT = 1
SLOTS = 32
QUAD = 4
BANK = 512
HOT_MAX = 1000


def is_hot(rows):
    return rows <= HOT_MAX and rows % ROWS == 0


def build(nc, dense_t, ids, hot_ids, tables, hot_tables, w1, b1, w2, b2, w3, out):
    nf = len(tables)
    nh = len(hot_tables)
    feats = nf + nh + 1
    batch = dense_t.shape[1]
    n_super = TILES * P
    n_half = n_super // HALVES
    tiles_half = TILES // HALVES
    supers = batch // n_super
    groups = P // QUAD
    assert n_super // QUAD == P and batch % n_super == 0 and 2 * n_half == BANK
    pairs = feats * (feats - 1) // 2
    kz = 117
    n_kz = pairs // kz
    assert kz * n_kz == pairs
    d1, d2 = w1.shape[1], w2.shape[1]
    m1, m2 = d1 // P, d2 // P
    hot_rows = hot_tables[0].shape[0]
    kh = hot_rows // ROWS
    assert kh <= P and all(t.shape[0] == hot_rows for t in hot_tables)

    turn_groups = [list(range(f, min(f + 4, nf))) for f in range(0, nf, 4)]
    n_turn = len(turn_groups)
    fills_half = nh + tiles_half * n_turn
    per_fill = BANK // (QUAD * feats)
    n_gram = groups // per_fill
    assert n_gram * per_fill == groups
    gram_half = tiles_half * n_gram
    pair_start = [q * feats - q * (q + 1) // 2 for q in range(feats)]
    col_groups = [list(range(q, min(q + 4, feats - 1))) for q in range(0, feats - 1, 4)]
    n_cols = len(col_groups)
    tail = ([("cols", g) for g in range(n_cols)] + [("zt", k) for k in range(n_kz)]
            + [("h1", m) for m in range(m1)] + [("h2", m) for m in range(m2)] + [("y", 0)])
    tail_count = {kind: len([1 for key in tail if key[0] == kind]) for kind in ("cols", "zt", "h1", "h2", "y")}
    tail_bank = {key: j % 2 for j, key in enumerate(tail)}
    tail_nth = {key: j // 2 for j, key in enumerate(tail)}
    tail_per = [len([j for j in range(len(tail)) if j % 2 == b]) for b in range(2)]
    parts = {"cols": 1, "zt": 1, "h1": n_kz + 1, "h2": m1, "y": 1}
    tail_steps = [("tail", key, part) for key in tail for part in range(parts[key[0]])]
    tail_cut = tail_steps.index(("tail", ("h1", 3), 0))

    items = HALVES * nh
    chunks = items * ROWS
    assert items % 2 == 0 and nh >= 5

    def plan(with_tail):
        steps = [("ids", 0)]
        for half in range(HALVES):
            tail_half = (tail_steps[:tail_cut] if half == 0 else tail_steps[tail_cut:]) if with_tail else []
            turns = [("turn", half * tiles_half + k, g) for k in range(tiles_half) for g in range(n_turn)]
            n = nh * ROWS
            for i in range(n):
                if i % ROWS == 0 and i // ROWS >= nh - 5:
                    steps += turns[:tiles_half]
                    turns = turns[tiles_half:]
                steps += tail_half[i * len(tail_half) // n:(i + 1) * len(tail_half) // n]
                at = half * n + i
                steps.append(("chunk", at))
                if (at + LEAD - 1) % (2 * ROWS) == 0 and at + LEAD < chunks:
                    steps.append(("ids", (at + LEAD) // (2 * ROWS)))
            steps += turns
            steps += [("gram", m) for m in range(half * gram_half, (half + 1) * gram_half)]
        return steps

    fill_steps = [("hot", s[1] // ROWS) if s[0] == "chunk" else s for s in plan(False)
                  if s[0] == "turn" or (s[0] == "chunk" and s[1] % ROWS == 0)]
    fill_no = {step: n for n, step in enumerate(fill_steps)}
    fills = len(fill_steps)
    assert fills == HALVES * fills_half

    with ExitStack() as ctx:
        def sb(name, shape, dt=F32):
            return ctx.enter_context(nc.sbuf_tensor(name, shape, dt))

        def psum(name, shape):
            return ctx.enter_context(nc.psum_tensor(name, shape, F32))

        def sem(name):
            return ctx.enter_context(nc.semaphore(name))

        ident = sb("ident", [P, P])
        ids_sb = [sb(f"ids_sb{k}", [P, nf], I32) for k in range(TILES)]
        raw = [sb(f"raw{k}", [P, nf, P]) for k in range(TILES)]
        xt = sb("xt", [P, n_half, SLOTS])
        dense_sb = sb("dense_sb", [P, batch])
        hot_hi = sb("hot_hi", [P, nh, ROWS, P], F32R)
        hot_lo = sb("hot_lo", [P, nh, ROWS, P], F32R)
        ids_row = sb("ids_row", [nh, batch], F32R)
        pick = sb("pick", [nh, nh, P], F32R)
        row_no = sb("row_no", [P, ROWS])
        onehot = sb("onehot", [P, RING, n_half], F32R)
        gram = sb("gram", [P, P, feats])
        z = sb("z", [P, QUAD, pairs])
        zt = sb("zt", [P, n_kz, n_super])
        h1 = sb("h1", [P, m1, n_super])
        h2 = sb("h2", [P, m2, n_super])
        w1z_sb = sb("w1z_sb", [P, n_kz, d1])
        w1d_sb = sb("w1d_sb", [P, d1])
        w2_sb = sb("w2_sb", [P, m1, d2])
        w3_sb = sb("w3_sb", [P, m2])
        b1_sb = sb("b1_sb", [P, m1])
        b2_sb = sb("b2_sb", [P, m2])
        hot_in = xt[:, :, :].rearrange("p b f -> p (b f)")[0:kh, 0:nh * ROWS * P].rearrange(
            "p (j r) -> p j r", j=nh)
        ids_row_in = h1[0:nh, :, :].rearrange("j m n -> j (m n)")[:, 0:batch].bitcast(I32)
        pick_in = z[0:nh, :, :].rearrange("j s c -> j (s c)")[:, 0:nh * P]

        x_ps = [psum(f"x_ps{b}", [P, BANK]) for b in range(3)]
        ids_ps = psum("ids_ps", [P, 2, n_half])
        gram_ps = [psum(f"gram_ps{b}", [P, BANK]) for b in range(2)]
        tail_ps = [psum(f"tail_ps{b}", [P, BANK]) for b in range(2)]

        slots_opened = sem("slots_opened")
        slot_ids_opened = sem("slot_ids_opened")
        ids_opened = sem("ids_opened")
        ids_in = [sem(f"ids_in{k}") for k in range(TILES)]
        rows_in = [[sem(f"rows_in{k}_{g}") for g in range(n_turn)] for k in range(TILES)]
        hot_landed = [sem(f"hot_landed{j}") for j in range(nh)]
        ids_row_landed = sem("ids_row_landed")
        dense_in = sem("dense_in")
        weights_in = sem("weights_in")
        ident_ready = sem("ident_ready")
        consts_ready = sem("consts_ready")
        hot_rounded = sem("hot_rounded")
        hot_split = sem("hot_split")
        ids_row_ready = sem("ids_row_ready")
        xt_cleared = sem("xt_cleared")
        ids_full = sem("ids_full")
        chunk_ready = sem("chunk_ready")
        chunk_used = sem("chunk_used")
        turn_full = [sem(f"turn_full{k}") for k in range(TILES)]
        x_copied = sem("x_copied")
        dense_copied = sem("dense_copied")
        gram_full = sem("gram_full")
        gram_act = sem("gram_act")
        gram_dve = sem("gram_dve")
        tail_full = {kind: sem(f"{kind}_full") for kind in tail_count}
        tail_copied = [sem(f"tail_copied{b}") for b in range(2)]
        y_stored = sem("y_stored")

        block = ctx.enter_context(nc.Block())

        def reach(eng, which, value):
            if not isinstance(value, int) or value > 0:
                eng.wait_ge(which, value)

        def gram_copy(eng, copy, done, quads, T, m):
            eng.wait_ge(gram_full, T * (HALVES * gram_half) + (m + 1))
            if m == 0:
                reach(eng, tail_full["cols"], 0 if isinstance(T, int) and T == 0 else T * n_cols + CREDIT)
            for s in quads:
                rows = slice(32 * s, 32 * s + 32)
                src = gram_ps[m % 2][rows, 0:per_fill * QUAD * feats].rearrange(
                    "p (g c) -> p g c", g=per_fill)[:, :, s * feats:(s + 1) * feats]
                last = copy(gram[rows, per_fill * m:per_fill * (m + 1), :], src)
            last.then_inc(done, 1)

        def tail_copy(eng, copy, bias_relu, T, key):
            kind, j = key
            bank = tail_bank[key]
            ps = tail_ps[bank]
            eng.wait_ge(tail_full[kind], T * tail_count[kind] + (j + 1 + CREDIT))
            if kind == "cols":
                for c, q in enumerate(col_groups[j]):
                    src = ps[:, c * P:(c + 1) * P].rearrange("g (s p) -> g s p", s=QUAD)[:, :, q + 1:feats]
                    last = copy(z[:, :, pair_start[q]:pair_start[q] + feats - 1 - q], src)
            elif kind == "zt":
                src = ps[0:kz, :].rearrange("p (s g) -> p g s", s=QUAD)
                last = copy(zt[0:kz, j, :].rearrange("p (g s) -> p g s", s=QUAD), src)
            elif kind == "h1":
                last = bias_relu(h1[:, j, :], ps[:, :], b1_sb[:, j:j + 1])
            elif kind == "h2":
                last = bias_relu(h2[:, j, :], ps[:, :], b2_sb[:, j:j + 1])
            else:
                last = copy(dense_sb[0:1, bass.ds(T * n_super, n_super)], ps[0:1, :])
            last.then_inc(tail_copied[bank], 1)

        @block.sync
        def _(sp):
            for k in range(TILES):
                sp.dma_start(ids_sb[k][:, :], ids[:, k, :]).then_inc(ids_in[k], 16)
            sp.dma_start(ids_row_in, hot_ids).then_inc(ids_row_landed, 16)
            for j in range(nh):
                sp.dma_start(hot_in[:, j, :], hot_tables[j].rearrange("(p c) d -> p (c d)", c=ROWS)).then_inc(
                    hot_landed[j], 16)
            sp.dma_start(dense_sb[:, :], dense_t).then_inc(dense_in, 16)
            sp.dma_start(w1z_sb[0:kz, :, :], w1[0:pairs, :].rearrange("(k p) n -> p k n", p=kz)).then_inc(weights_in, 16)
            sp.dma_start(w1d_sb[:, :], w1[pairs:pairs + P, :]).then_inc(weights_in, 16)
            sp.dma_start(w2_sb[:, :, :], w2.rearrange("(k p) n -> p k n", p=P)).then_inc(weights_in, 16)
            sp.dma_start(w3_sb[:, :], w3).then_inc(weights_in, 16)
            sp.dma_start(b1_sb[:, :], b1).then_inc(weights_in, 16)
            sp.dma_start(b2_sb[:, :], b2).then_inc(weights_in, 16)
            with sp.Fori(1, supers) as T:
                for k in range(TILES):
                    sp.wait_ge(turn_full[k], T * n_turn)
                    sp.sem_inc(slot_ids_opened, 1)
                    sp.dma_start(ids_sb[k][:, :], ids[:, bass.ds(T * TILES + k, 1), :].rearrange(
                        "p o f -> p (o f)")).then_inc(ids_in[k], 16)

        @block.gpsimd
        def _(pool):
            nc.gpsimd.memset(ident[:, :], 0.0).then_inc(consts_ready, 1)
            nc.gpsimd.memset(pick_in, 0.0).then_inc(consts_ready, 1)
            pool.wait_ge(consts_ready, 2)
            nc.gpsimd.affine_select(out=ident[:, :], in_=ident[:, :], compare_op=ALU.not_equal, fill=1.0, base=0,
                                    pattern=[[-1, P]], channel_multiplier=1).then_inc(ident_ready, 1)
            pick3 = pick_in.rearrange("j (k p) -> j k p", k=nh)
            nc.gpsimd.affine_select(out=pick3, in_=pick3, compare_op=ALU.not_equal, fill=1.0, base=0,
                                    pattern=[[-1, nh], [0, P]], channel_multiplier=1).then_inc(consts_ready, 1)
            nc.gpsimd.iota(row_no[:, :], pattern=[[1, ROWS]], base=0, channel_multiplier=ROWS,
                           allow_small_or_imprecise_dtypes=True).then_inc(consts_ready, 1)

            def gathers(T):
                for k in range(TILES):
                    pool.wait_ge(ids_in[k], (T + 1) * 16)
                    reach(pool, turn_full[k], T * n_turn)
                    pool.sem_inc(slots_opened, 1)
                    for g, fs in enumerate(turn_groups):
                        for f in fs:
                            nc.gpsimd.indirect_dma_start(
                                out=raw[k][:, f, :], out_offset=None, in_=tables[f],
                                in_offset=bass.IndirectOffsetOnAxis(ap=ids_sb[k][:, f:f + 1], axis=0),
                            ).then_inc(rows_in[k][g], 16)

            gathers(0)
            with pool.Fori(1, supers) as T:
                gathers(T)

        @block.tensor
        def _(pe):
            def x_free(T, n):
                reach(pe, x_copied, T * fills + (n - (len(x_ps) - 1) if n > 0 else 0))
                return x_ps[n % len(x_ps)]

            def turn_rows(T, k, g):
                pe.wait_ge(rows_in[k][g], (T + 1) * (16 * len(turn_groups[g])))
                ps = x_free(T, fill_no["turn", k, g])
                for c, f in enumerate(turn_groups[g]):
                    last = nc.tensor.transpose(ps[:, c * P:(c + 1) * P], raw[k][:, f, :], ident[:, :])
                last.then_inc(turn_full[k], 1)

            def hot_ids_spread(T, pair):
                reach(pe, chunk_ready, T * chunks + pair * 2 * ROWS)
                pe.sem_inc(ids_opened, 1)
                for i in range(2):
                    half, j = divmod(2 * pair + i, nh)
                    last = nc.tensor.matmul(ids_ps[:, i, :], pick[:, j, :],
                                            ids_row[:, bass.ds(T * n_super + half * n_half, n_half)],
                                            start=True, stop=True)
                last.then_inc(ids_full, 1)

            def hot_chunk(T, at):
                item, c = divmod(at, ROWS)
                j = item % nh
                n = fill_no["hot", item]
                ps = (x_free(T, n) if c == 0 else x_ps[n % len(x_ps)])[:, 0:n_half]
                pe.wait_ge(chunk_ready, T * chunks + (at + 1))
                for table in (hot_hi, hot_lo):
                    last = nc.tensor.matmul(ps, table[0:kh, j, c, :], onehot[0:kh, at % RING, :],
                                            start=(c == 0 and table is hot_hi), stop=(c == ROWS - 1 and table is hot_lo))
                last.then_inc(chunk_used, 1)

            def products(T, m):
                for done in (gram_act, gram_dve):
                    reach(pe, done, T * (HALVES * gram_half) + (m - 1))
                for g in range(per_fill):
                    b = ((m % gram_half) * per_fill + g) * QUAD
                    col = g * QUAD * feats
                    last = nc.tensor.matmul(gram_ps[m % 2][:, col:col + QUAD * feats],
                                            xt[:, b:b + QUAD, :].rearrange("p b f -> p (b f)"),
                                            xt[:, b:b + QUAD, 0:feats], start=True, stop=True)
                last.then_inc(gram_full, 1)

            def tail_has(kind, T):
                for b in range(2):
                    nth = [tail_nth[key] for key in tail if key[0] == kind and tail_bank[key] == b]
                    if nth:
                        pe.wait_ge(tail_copied[b], T * tail_per[b] + (max(nth) + 1 + CREDIT))

            def tail_step(T, key, part):
                kind, j = key
                bank = tail_bank[key]
                ps = tail_ps[bank]
                if part == 0:
                    if j == 0:
                        if kind == "cols":
                            for done in (gram_act, gram_dve):
                                pe.wait_ge(done, T * (HALVES * gram_half) + HALVES * gram_half)
                        else:
                            tail_has({"zt": "cols", "h1": "zt", "h2": "h1", "y": "h2"}[kind], T)
                    pe.wait_ge(tail_copied[bank], T * tail_per[bank] + (tail_nth[key] + CREDIT))
                if kind == "cols":
                    for c, q in enumerate(col_groups[j]):
                        last = nc.tensor.transpose(ps[:, c * P:(c + 1) * P], gram[:, :, q], ident[:, :])
                elif kind == "zt":
                    for s in range(QUAD):
                        last = nc.tensor.transpose(ps[0:kz, s * P:(s + 1) * P], z[:, s, j * kz:(j + 1) * kz],
                                                   ident[:, :])
                elif kind == "h1":
                    w = slice(j * P, (j + 1) * P)
                    if part == 0:
                        last = nc.tensor.matmul(ps[:, :], w1d_sb[:, w], dense_sb[:, bass.ds(T * n_super, n_super)],
                                                start=True, stop=False)
                    else:
                        last = nc.tensor.matmul(ps[:, :], w1z_sb[0:kz, part - 1, w], zt[0:kz, part - 1, :],
                                                start=False, stop=(part == n_kz))
                elif kind == "h2":
                    last = nc.tensor.matmul(ps[:, :], w2_sb[:, part, j * P:(j + 1) * P], h1[:, part, :],
                                            start=(part == 0), stop=(part == m1 - 1))
                else:
                    for c in range(m2):
                        last = nc.tensor.matmul(ps[0:1, :], w3_sb[:, c:c + 1], h2[:, c, :],
                                                start=(c == 0), stop=(c == m2 - 1))
                if part == parts[kind] - 1:
                    last.then_inc(tail_full[kind], 1)

            def super_tile(T, with_tail):
                for kind, *what in plan(with_tail):
                    if kind == "ids":
                        hot_ids_spread(T, *what)
                    elif kind == "chunk":
                        hot_chunk(T, *what)
                    elif kind == "turn":
                        turn_rows(T, *what)
                    elif kind == "tail":
                        tail_step(T - 1, *what)
                    else:
                        half, first = divmod(what[0], gram_half)
                        if first == 0:
                            pe.wait_ge(x_copied, T * fills + (half + 1) * fills_half)
                            pe.wait_ge(dense_copied, T * HALVES + (half + 1))
                        products(T, *what)

            for full in tail_full.values():
                pe.sem_inc(full, CREDIT)
            pe.wait_ge(ident_ready, 1)
            pe.wait_ge(ids_row_ready, 2)
            pe.wait_ge(hot_rounded, nh)
            pe.wait_ge(hot_split, nh)
            pe.wait_ge(xt_cleared, 1)
            pe.wait_ge(weights_in, 6 * 16)
            pe.wait_ge(dense_in, 16)
            super_tile(0, False)
            with pe.Fori(1, supers) as T:
                super_tile(T, True)
            for _, key, part in tail_steps:
                tail_step(supers - 1, key, part)

        @block.scalar
        def _(act):
            copy = nc.scalar.copy

            def bias_relu(o, i, b):
                return nc.scalar.activation(o, i, ACT.Relu, bias=b)

            def super_tile(T, with_tail):
                for kind, *what in plan(with_tail):
                    if kind == "chunk":
                        item, c = divmod(what[0], ROWS)
                        half, j = divmod(item, nh)
                        if c == ROWS - 1:
                            act.wait_ge(chunk_used, T * chunks + (what[0] + 1))
                            n = fill_no["hot", item]
                            copy(xt[:, :, nf + j], x_ps[n % len(x_ps)][:, 0:n_half]).then_inc(x_copied, 1)
                            if j == 0:
                                copy(xt[:, :, nf + nh], dense_sb[:, bass.ds(T * n_super + half * n_half, n_half)]
                                     ).then_inc(dense_copied, 1)
                    elif kind == "turn":
                        k, g = what
                        fs = turn_groups[g]
                        act.wait_ge(turn_full[k], T * n_turn + (g + 1))
                        n = fill_no["turn", k, g]
                        b = (k % tiles_half) * P
                        src = x_ps[n % len(x_ps)][:, 0:len(fs) * P].rearrange("p (f b) -> p b f", b=P)
                        copy(xt[:, b:b + P, fs[0]:fs[-1] + 1], src).then_inc(x_copied, 1)
                    elif kind == "tail":
                        key, part = what
                        if tail_bank[key] == 0 and part == parts[key[0]] - 1:
                            tail_copy(act, copy, bias_relu, T - 1, key)
                    elif kind == "gram":
                        gram_copy(act, copy, gram_act, (0, 1), T, *what)

            act.sem_inc(tail_copied[0], CREDIT)
            for j in range(nh):
                act.wait_ge(hot_landed[j], 16)
                copy(hot_hi[0:kh, j, :, :].rearrange("p c d -> p (c d)"), hot_in[:, j, :]).then_inc(hot_rounded, 1)
            act.wait_ge(xt_cleared, 1)
            act.wait_ge(dense_in, 16)
            act.wait_ge(weights_in, 6 * 16)
            super_tile(0, False)
            with act.Fori(1, supers) as T:
                super_tile(T, True)
            for key in tail:
                if tail_bank[key] == 0:
                    tail_copy(act, copy, bias_relu, supers - 1, key)
            act.wait_ge(tail_copied[0], supers * tail_per[0] + CREDIT)
            act.dma_start(out, dense_sb[0:1, :]).then_inc(y_stored, 16)
            act.wait_ge(y_stored, 16)

        @block.vector
        def _(dve):
            copy = nc.vector.tensor_copy

            def bias_relu(o, i, b):
                return nc.vector.tensor_scalar(o, i, b, 0.0, ALU.add, ALU.max)

            def make_chunk(T, at):
                item, c = divmod(at, ROWS)
                if at % (2 * ROWS) == 0:
                    dve.wait_ge(ids_full, T * (items // 2) + (item // 2 + 1))
                reach(dve, chunk_used, T * chunks + (at + 1 - RING))
                nc.vector.tensor_scalar(onehot[0:kh, at % RING, :], ids_ps[0:kh, item % 2, :],
                                        row_no[0:kh, c:c + 1], None, ALU.is_equal).then_inc(chunk_ready, 1)

            def super_tile(T, with_tail):
                for kind, *what in plan(with_tail):
                    if kind == "chunk":
                        if what[0] == 0:
                            for at in range(LEAD):
                                make_chunk(T, at)
                        if what[0] + LEAD < chunks:
                            make_chunk(T, what[0] + LEAD)
                    elif kind == "tail":
                        key, part = what
                        if tail_bank[key] == 1 and part == parts[key[0]] - 1:
                            tail_copy(dve, copy, bias_relu, T - 1, key)
                    elif kind == "gram":
                        gram_copy(dve, copy, gram_dve, (2, 3), T, *what)

            dve.sem_inc(tail_copied[1], CREDIT)
            dve.wait_ge(ids_row_landed, 16)
            copy(ids_row[:, :], ids_row_in).then_inc(ids_row_ready, 1)
            dve.wait_ge(consts_ready, 4)
            copy(pick[:, :, :].rearrange("j k p -> j (k p)"), pick_in).then_inc(ids_row_ready, 1)
            for j in range(nh):
                dve.wait_ge(hot_rounded, j + 1)
                nc.vector.tensor_tensor(hot_lo[0:kh, j, :, :].rearrange("p c d -> p (c d)"), hot_in[:, j, :],
                                        hot_hi[0:kh, j, :, :].rearrange("p c d -> p (c d)").bitcast(F32),
                                        ALU.subtract).then_inc(hot_split, 1)
            dve.wait_ge(hot_split, nh)
            nc.vector.memset(xt[:, :, feats:], 0.0).then_inc(xt_cleared, 1)
            dve.wait_ge(weights_in, 6 * 16)
            super_tile(0, False)
            with dve.Fori(1, supers) as T:
                super_tile(T, True)
            for key in tail:
                if tail_bank[key] == 1:
                    tail_copy(dve, copy, bias_relu, supers - 1, key)


def kernel(**inputs):
    import numpy as np
    import concourse.bacc as bacc
    from concourse.bass_utils import run_bass_kernel_spmd

    batch, n_tables = inputs["ids"].shape
    hot = [f for f in range(n_tables) if is_hot(inputs[f"tbl_{f}"].shape[0])]
    cold = [f for f in range(n_tables) if f not in hot]
    order = cold + hot + [n_tables]
    start = [i * (n_tables + 1) - i * (i + 1) // 2 for i in range(n_tables + 1)]
    pair_rows = [start[min(a, b)] + abs(a - b) - 1 for n, a in enumerate(order) for b in order[n + 1:]]
    w1 = np.asarray(inputs["W_top1"])
    ids = np.asarray(inputs["ids"])
    arrays = {
        "dense_t": inputs["r_dense_x"].T,
        "ids": ids[:, cold].reshape(batch // P, P, len(cold)).transpose(1, 0, 2),
        "hot_ids": ids[:, hot].T,
        "w1": np.concatenate([w1[pair_rows], w1[len(pair_rows):]]),
        "b1": np.asarray(inputs["b_top1"]).reshape(-1, P).T,
        "w2": inputs["W_top2"],
        "b2": np.asarray(inputs["b_top2"]).reshape(-1, P).T,
        "w3": np.asarray(inputs["W_top3"]).reshape(-1, P).T,
    }
    for f in range(n_tables):
        arrays[f"tbl_{f}"] = inputs[f"tbl_{f}"]
    arrays = {n: np.ascontiguousarray(a) for n, a in arrays.items()}
    nc = bacc.Bacc("TRN2", target_bir_lowering=False, num_devices=1)
    ap = {n: nc.dram_tensor(f"in_{n}", a.shape, mybir.dt.from_np(a.dtype), kind="ExternalInput").ap()
          for n, a in arrays.items()}
    y = nc.dram_tensor("y_out", (1, batch), F32, kind="ExternalOutput").ap()
    build(nc, ap["dense_t"], ap["ids"], ap["hot_ids"], [ap[f"tbl_{f}"] for f in cold], [ap[f"tbl_{f}"] for f in hot],
          ap["w1"], ap["b1"], ap["w2"], ap["b2"], ap["w3"], y)
    r = run_bass_kernel_spmd(nc, [{f"in_{n}": a for n, a in arrays.items()}], core_ids=[0])
    return r.results[0]["y_out"].reshape(batch, 1)
```

```python
from contextlib import ExitStack

import concourse.bass as bass
from concourse import mybir
from concourse.alu_op_type import AluOpType as ALU

F32 = mybir.dt.float32
F32R = mybir.dt.float32r
I32 = mybir.dt.int32
ACT = mybir.ActivationFunctionType

P = 128
TILES = 4
HALVES = 2
ROWS = 8
RING = 8
LEAD = 7
SLACK = 2
COVER = {"cols": 2.0, "zt": 1.0, "h1": 0.2, "h2": 0.15, "y": 0.25}
COVER_STAGE = 2.5
COVER_START = 1.5
SPREAD = 1.2
SLOTS = 32
QUAD = 4
BANK = 512
HOT = 6


def build(nc, dense_t, ids, hot_ids, tables, hot_tables, w1, b1, w2, b2, w3, out):
    nf = len(tables)
    nh = len(hot_tables)
    feats = nf + nh + 1
    batch = dense_t.shape[1]
    n_super = TILES * P
    n_half = n_super // HALVES
    tiles_half = TILES // HALVES
    supers = batch // n_super
    groups = P // QUAD
    assert batch % n_super == 0 and 2 * n_half == BANK
    pairs = feats * (feats - 1) // 2
    d1, d2 = w1.shape[1], w2.shape[1]
    m1, m2 = d1 // P, d2 // P
    hot_rows = hot_tables[0].shape[0]
    kh = hot_rows // ROWS
    assert kh <= P and all(t.shape[0] == hot_rows for t in hot_tables)

    turn_groups = [list(range(f, min(f + 4, nf))) for f in range(0, nf, 4)]
    n_turn = len(turn_groups)
    fills_half = nh + tiles_half * n_turn
    per_fill = BANK // (QUAD * feats)
    n_gram = groups // per_fill
    assert n_gram * per_fill == groups
    gram_half = tiles_half * n_gram
    groups_half = tiles_half * groups
    half_pairs, pair_start = [0, 0], []
    for q in range(feats - 1):
        pair_start.append(half_pairs[q % 2])
        half_pairs[q % 2] += feats - 1 - q
    col_groups = [list(range(q, min(q + 8, feats - 1), 2)) for q in range(0, feats - 1, 8)]
    assert 2 * groups_half == P and (feats - 1) % 2 == 0
    rest = 64
    z_blocks = [[(0, slice(0, half_pairs[0] - rest))], [(1, slice(0, P))],
                [(1, slice(P - rest, half_pairs[1])), (0, slice(half_pairs[0] - rest, half_pairs[0]))]]
    n_kz = len(z_blocks)
    kz = [block[0][1].stop - block[0][1].start for block in z_blocks]
    assert sum(kz) == pairs and max(kz) <= P
    n_cols = len(col_groups)
    tail = ([("cols", g) for g in range(n_cols)] + [("zt", k) for k in range(n_kz)]
            + [("h1", m) for m in range(m1)] + [("h2", m) for m in range(m2)] + [("y", 0)])
    tail_count = {kind: len([1 for key in tail if key[0] == kind]) for kind in ("cols", "zt", "h1", "h2", "y")}
    tail_bank = {key: j % 2 for j, key in enumerate(tail)}
    tail_nth = {key: j // 2 for j, key in enumerate(tail)}
    tail_per = [len([j for j in range(len(tail)) if j % 2 == b]) for b in range(2)]
    layer = {kind: [(part, "hi", k) for k in range(n) for part in ("hi", "lo")]
             + [("hi", "lo", k) for k in range(n)] for kind, n in (("h1", n_kz), ("h2", m1))}
    layer["h1"].insert(0, ("w", "x", 0))
    parts = {"cols": 1, "zt": 1, "h1": -(-len(layer["h1"]) // 2), "h2": -(-len(layer["h2"]) // 2), "y": 1}
    tail_steps = [("tail", key, part) for key in tail for part in range(parts[key[0]])]

    items = HALVES * nh
    early = 2 * ROWS
    chunks = items * ROWS
    assert items % 2 == 0 and nh * ROWS > 2 * early

    def chunk_steps(at):
        step = [("chunk", at)]
        if (at + LEAD - SLACK) % (2 * ROWS) == 0:
            step.append(("ids", (at + LEAD - SLACK) // (2 * ROWS)))
        return step

    def made_at(at):
        return [c for c in range(at, at + LEAD + 1) if at == max(c, c // (2 * ROWS) * (2 * ROWS) + SLACK) - LEAD]

    first_steps = [("ids", 0)] + [step for at in range(early) for step in chunk_steps(at)]

    def plan(first, last):
        steps = []
        for half in range(HALVES):
            tail_half = [] if first and half == 0 else [(*step, half) for step in tail_steps]
            turns = [[("turn", half * tiles_half + k, g) for g in range(n_turn)] for k in range(tiles_half)]
            n = nh * ROWS - early
            tail_at = [COVER_START]
            for _, key, part, *_ in tail_half:
                ends = part == parts[key[0]] - 1 and key[1] == tail_count[key[0]] - 1
                tail_at.append(tail_at[-1] + (COVER_STAGE if ends else COVER[key[0]]))
            scale = SPREAD * n / tail_at[-1] if tail_half else 0
            turn_at = [(i * (n // ROWS) // n_turn + 1) * ROWS - 1 for i in range(n_turn)]
            for i in range(n):
                steps += [step for step, at in zip(tail_half, tail_at) if i - 1 < at * scale <= i]
                steps += chunk_steps(half * nh * ROWS + early + i)
                steps += [turn for turn, at in zip(turns[0], turn_at) if at == i]
            steps += [step for step, at in zip(tail_half, tail_at) if at * scale > n - 1]
            assert len([s for s in steps if s[0] == "tail" and s[3] == half]) == len(tail_half)
            m = half * gram_half
            for i in range(n_gram):
                steps += turns[1][i * n_turn // n_gram:(i + 1) * n_turn // n_gram]
                steps.append(("gram", m + i))
            m += n_gram
            at = (half + 1) * nh * ROWS
            for i in range(n_gram):
                steps.append(("gram", m + i))
                if half == 0 or not last:
                    for c in range(i * early // n_gram, (i + 1) * early // n_gram):
                        steps += chunk_steps(at + c)
            steps.append(("xt free",))
        return [step for step in steps if not last or step != ("ids", items // 2)]

    fill_steps = [("hot", s[1] // ROWS) if s[0] == "chunk" else s for s in first_steps + plan(True, True)
                  if s[0] == "turn" or (s[0] == "chunk" and s[1] % ROWS == 0)]
    fill_no = {step: n for n, step in enumerate(fill_steps)}
    fills = len(fill_steps)
    assert fills == HALVES * fills_half

    with ExitStack() as ctx:
        def sb(name, shape, dt=F32):
            return ctx.enter_context(nc.sbuf_tensor(name, shape, dt))

        def psum(name, shape):
            return ctx.enter_context(nc.psum_tensor(name, shape, F32))

        def sem(name):
            return ctx.enter_context(nc.semaphore(name))

        ident = sb("ident", [P, P])
        ids_sb = [sb(f"ids_sb{k}", [P, nf], I32) for k in range(TILES)]
        raw = [sb(f"raw{k}", [P, nf, P]) for k in range(TILES)]
        xt = sb("xt", [P, n_half, SLOTS])
        dense_sb = sb("dense_sb", [P, batch])
        hot_hi = sb("hot_hi", [P, nh, ROWS, P], F32R)
        hot_lo = sb("hot_lo", [P, nh, ROWS, P], F32R)
        ids_row = sb("ids_row", [nh, batch], F32R)
        pick = sb("pick", [nh, nh, P], F32R)
        row_no = sb("row_no", [P, ROWS])
        onehot = sb("onehot", [P, RING, n_half], F32R)
        gram = sb("gram", [P, feats - 1, groups_half])
        z = sb("z", [P, QUAD, half_pairs[0]])
        zt = sb("zt", [P, n_kz, n_half])
        zt_hi = sb("zt_hi", [P, n_kz, n_half], F32R)
        zt_lo = sb("zt_lo", [P, n_kz, n_half], F32R)
        h1 = sb("h1", [P, m1, n_half])
        h1_hi = sb("h1_hi", [P, m1, n_half], F32R)
        h1_lo = sb("h1_lo", [P, m1, n_half], F32R)
        h2 = sb("h2", [P, m2, n_half])
        w1z_hi = sb("w1z_hi", [P, n_kz, d1], F32R)
        w1z_lo = sb("w1z_lo", [P, n_kz, d1], F32R)
        w1d_sb = sb("w1d_sb", [P, d1])
        w2_hi = sb("w2_hi", [P, m1, d2], F32R)
        w2_lo = sb("w2_lo", [P, m1, d2], F32R)
        w3_sb = sb("w3_sb", [P, m2])
        b1_sb = sb("b1_sb", [P, m1])
        b2_sb = sb("b2_sb", [P, m2])
        hot_in = [buf[0:kh, n * ROWS:(n + 1) * ROWS, :].rearrange("p a b -> p (a b)")
                  for buf, count in ((raw[1], 2), (raw[2], 2), (raw[3], 2)) for n in range(count)]
        assert len(hot_in) >= nh
        ids_row_in = dense_sb[0:nh, :].bitcast(I32)
        w1z_in = [h1[:, 0:2, :], h1[:, 2:4, :], h2[:, :, :]]
        w2_in = [z[:, :, :].rearrange("p s c -> p (s c)")[:, 0:2 * d2],
                 zt[:, :, :].rearrange("p k n -> p (k n)")[:, 0:2 * d2]]
        assert m1 == 4 and m2 == 2 and n_half * 2 == d1
        weight_parts = [(w1z_hi[0:n, k, :], w1z_lo[0:n, k, :], w1z_in[k][0:n, :, :].rearrange("p m n -> p (m n)"))
                        for k, n in enumerate(kz)]
        weight_parts += [(*(part[:, 2 * k:2 * k + 2, :].rearrange("p k n -> p (k n)") for part in (w2_hi, w2_lo)), w2_in[k])
                         for k in range(2)]
        pick_in = gram[0:nh, :, :].rearrange("j q g -> j (q g)")[:, 0:nh * P]

        x_ps = [psum(f"x_ps{b}", [P, BANK]) for b in range(3)]
        ids_ps = psum("ids_ps", [P, 2, n_half])
        gram_ps = [psum(f"gram_ps{b}", [P, BANK]) for b in range(2)]
        tail_ps = [psum(f"tail_ps{b}", [P, BANK]) for b in range(2)]

        slots_opened = sem("slots_opened")
        slot_ids_opened = sem("slot_ids_opened")
        ids_opened = sem("ids_opened")
        stages_opened = sem("stages_opened")
        ids_in = [sem(f"ids_in{k}") for k in range(TILES)]
        rows_in = [[sem(f"rows_in{k}_{g}") for g in range(n_turn)] for k in range(TILES)]
        hot_landed = [sem(f"hot_landed{j}") for j in range(nh)]
        ids_row_landed = sem("ids_row_landed")
        dense_in = sem("dense_in")
        weights_in = sem("weights_in")
        weights_rounded = sem("weights_rounded")
        weights_split = sem("weights_split")
        even_copied = sem("even_copied")
        odd_copied = sem("odd_copied")
        rest_turned = sem("rest_turned")
        zt_rounded = sem("zt_rounded")
        zt_split = sem("zt_split")
        h1_rounded = sem("h1_rounded")
        h1_split = sem("h1_split")
        ident_ready = sem("ident_ready")
        consts_ready = sem("consts_ready")
        hot_rounded = sem("hot_rounded")
        hot_split = sem("hot_split")
        ids_row_ready = sem("ids_row_ready")
        xt_cleared = sem("xt_cleared")
        ids_full = sem("ids_full")
        chunk_ready = sem("chunk_ready")
        chunk_used = sem("chunk_used")
        turn_full = [sem(f"turn_full{k}") for k in range(TILES)]
        x_copied = sem("x_copied")
        dense_copied = sem("dense_copied")
        gram_full = sem("gram_full")
        gram_act = sem("gram_act")
        gram_dve = sem("gram_dve")
        tail_full = {kind: sem(f"{kind}_full") for kind in tail_count}
        tail_copied = [sem(f"tail_copied{b}") for b in range(2)]
        y_stored = sem("y_stored")

        block = ctx.enter_context(nc.Block())

        def reach(eng, which, value):
            if not isinstance(value, int) or value > 0:
                eng.wait_ge(which, value)

        def gram_copy(eng, copy, done, quads, T, m):
            eng.wait_ge(gram_full, T * (HALVES * gram_half) + (m + 1))
            if m % gram_half == 0:
                reach(eng, tail_full["cols"], T * (HALVES * n_cols) + m // gram_half * n_cols)
            for s in quads:
                rows = slice(32 * s, 32 * s + 32)
                src = gram_ps[m % 2][rows, 0:per_fill * QUAD * feats].rearrange(
                    "p (g c) -> p c g", g=per_fill)[:, s * feats:(s + 1) * feats - 1, :]
                last = copy(gram[rows, :, per_fill * (m % gram_half):per_fill * (m % gram_half + 1)], src)
            last.then_inc(done, 1)

        def counted(T, half, per_half, more):
            return T * (HALVES * per_half) + ((half - 1) * per_half + more)

        def pairs_copy(copy, j, h):
            rows = slice(h * groups_half, (h + 1) * groups_half)
            for c, even in enumerate(col_groups[j]):
                q = even + h
                src = tail_ps[tail_bank["cols", j]][rows, c * P:(c + 1) * P].rearrange(
                    "g (s p) -> g s p", s=QUAD)[:, :, q + 1:feats]
                last = copy(z[rows, :, pair_start[q]:pair_start[q] + feats - 1 - q], src)
            return last

        def tail_copy(act, T, half, key):
            copy = nc.scalar.copy
            kind, j = key
            bank = tail_bank[key]
            ps = tail_ps[bank]
            act.wait_ge(tail_full[kind], counted(T, half, tail_count[kind], j + 1))
            if kind == "cols":
                last = pairs_copy(copy, j, 0)
                if isinstance(T, int) and T == supers:
                    last.then_inc(even_copied, 1)
                    act.wait_ge(even_copied, j + 1)
                    act.wait_ge(odd_copied, j + 1)
                    act.sem_inc(tail_copied[bank], 1)
                    return
                last = pairs_copy(copy, j, 1)
            elif kind == "zt":
                src = ps[0:kz[j], 0:n_half].rearrange("p (s g) -> p g s", s=QUAD)
                copy(zt_hi[0:kz[j], j, :].rearrange("p (g s) -> p g s", s=QUAD), src).then_inc(zt_rounded, 1)
                last = copy(zt[0:kz[j], j, :].rearrange("p (g s) -> p g s", s=QUAD), src)
            elif kind == "h1":
                bias = b1_sb[:, j:j + 1]
                nc.scalar.activation(h1_hi[:, j, :], ps[:, 0:n_half], ACT.Relu, bias=bias).then_inc(h1_rounded, 1)
                last = nc.scalar.activation(h1[:, j, :], ps[:, 0:n_half], ACT.Relu, bias=bias)
            elif kind == "h2":
                last = nc.scalar.activation(h2[:, j, :], ps[:, 0:n_half], ACT.Relu, bias=b2_sb[:, j:j + 1])
            else:
                last = copy(dense_sb[0:1, bass.ds(counted(T, half, n_half, 0), n_half)], ps[0:1, 0:n_half])
            last.then_inc(tail_copied[bank], 1)

        def tail_split(dve, T, half, key):
            kind, j = key
            if kind in ("zt", "h1"):
                bank = tail_bank[key]
                dve.wait_ge(tail_copied[bank], counted(T, half, tail_per[bank], tail_nth[key] + 1))
                rows, whole, hi, lo, split = ((kz[j], zt, zt_hi, zt_lo, zt_split) if kind == "zt" else
                                              (P, h1, h1_hi, h1_lo, h1_split))
                nc.vector.tensor_tensor(lo[0:rows, j, :], whole[0:rows, j, :], hi[0:rows, j, :].bitcast(F32),
                                        ALU.subtract).then_inc(split, 1)

        @block.sync
        def _(sp):
            sp.dma_start(ids_sb[0][:, :], ids[:, 0, :]).then_inc(ids_in[0], 16)
            sp.dma_start(ids_row_in, hot_ids).then_inc(ids_row_landed, 16)
            for j in range(nh):
                if 0 < j < TILES:
                    sp.dma_start(ids_sb[j][:, :], ids[:, j, :]).then_inc(ids_in[j], 16)
                sp.dma_start(hot_in[j], hot_tables[j].rearrange("(p c) d -> p (c d)", c=ROWS)).then_inc(
                    hot_landed[j], 16)
            sp.wait_ge(ids_row_ready, 1)
            sp.dma_start(dense_sb[:, :], dense_t).then_inc(dense_in, 16)
            for k, n in enumerate(kz):
                sp.dma_start(w1z_in[k][0:n, :, :].rearrange("p m n -> p (m n)"),
                             w1[sum(kz[:k]):sum(kz[:k + 1]), :]).then_inc(weights_in, 16)
            sp.dma_start(w1d_sb[:, :], w1[pairs:pairs + P, :]).then_inc(weights_in, 16)
            sp.dma_start(w3_sb[:, :], w3).then_inc(weights_in, 16)
            sp.dma_start(b1_sb[:, :], b1).then_inc(weights_in, 16)
            sp.dma_start(b2_sb[:, :], b2).then_inc(weights_in, 16)
            for k in range(2):
                sp.dma_start(w2_in[k].rearrange("p (k n) -> p k n", k=2),
                             w2.rearrange("(k p) n -> p k n", p=P)[:, 2 * k:2 * k + 2, :]).then_inc(weights_in, 16)
            with sp.Fori(1, supers) as T:
                for k in range(TILES):
                    sp.wait_ge(turn_full[k], T * n_turn)
                    sp.sem_inc(slot_ids_opened, 1)
                    sp.dma_start(ids_sb[k][:, :], ids[:, bass.ds(T * TILES + k, 1), :].rearrange(
                        "p o f -> p (o f)")).then_inc(ids_in[k], 16)

        @block.gpsimd
        def _(pool):
            nc.gpsimd.memset(ident[:, :], 0.0).then_inc(consts_ready, 1)
            nc.gpsimd.memset(pick_in, 0.0).then_inc(consts_ready, 1)
            pool.wait_ge(consts_ready, 2)
            nc.gpsimd.affine_select(out=ident[:, :], in_=ident[:, :], compare_op=ALU.not_equal, fill=1.0, base=0,
                                    pattern=[[-1, P]], channel_multiplier=1).then_inc(ident_ready, 1)
            pick3 = pick_in.rearrange("j (k p) -> j k p", k=nh)
            nc.gpsimd.affine_select(out=pick3, in_=pick3, compare_op=ALU.not_equal, fill=1.0, base=0,
                                    pattern=[[-1, nh], [0, P]], channel_multiplier=1).then_inc(consts_ready, 1)
            nc.gpsimd.iota(row_no[:, :], pattern=[[1, ROWS]], base=0, channel_multiplier=ROWS,
                           allow_small_or_imprecise_dtypes=True).then_inc(consts_ready, 1)

            def gathers(T):
                for k in range(TILES):
                    pool.wait_ge(ids_in[k], (T + 1) * 16)
                    reach(pool, turn_full[k], T * n_turn)
                    if isinstance(T, int) and k > 0:
                        pool.wait_ge(hot_split, min(2 * k, nh))
                    pool.sem_inc(slots_opened, 1)
                    for g, fs in enumerate(turn_groups):
                        for f in fs:
                            nc.gpsimd.indirect_dma_start(
                                out=raw[k][:, f, :], out_offset=None, in_=tables[f],
                                in_offset=bass.IndirectOffsetOnAxis(ap=ids_sb[k][:, f:f + 1], axis=0),
                            ).then_inc(rows_in[k][g], 16)

            gathers(0)
            with pool.Fori(1, supers) as T:
                gathers(T)

        @block.tensor
        def _(pe):
            def x_free(T, n):
                reach(pe, x_copied, T * fills + (n - (len(x_ps) - 1) if n > 0 else 0))
                return x_ps[n % len(x_ps)]

            def turn_rows(T, k, g):
                pe.wait_ge(rows_in[k][g], (T + 1) * (16 * len(turn_groups[g])))
                ps = x_free(T, fill_no["turn", k, g])
                for c, f in enumerate(turn_groups[g]):
                    last = nc.tensor.transpose(ps[:, c * P:(c + 1) * P], raw[k][:, f, :], ident[:, :])
                last.then_inc(turn_full[k], 1)

            def hot_ids_spread(T, pair):
                reach(pe, chunk_ready, T * chunks + pair * 2 * ROWS)
                pe.sem_inc(ids_opened, 1)
                for i in range(2):
                    half, j = divmod(2 * pair + i, nh)
                    last = nc.tensor.matmul(ids_ps[:, i, :], pick[:, j, :],
                                            ids_row[:, bass.ds(T * n_super + half * n_half, n_half)],
                                            start=True, stop=True)
                last.then_inc(ids_full, 1)

            def hot_chunk(T, at):
                item, c = divmod(at, ROWS)
                half, j = divmod(item, nh)
                n = fill_no["hot", item]
                ps = (x_free(T, n) if c == 0 else x_ps[n % len(x_ps)])[:, 0:n_half]
                if isinstance(T, int) and T == 0 and half == 0 and c == 0:
                    pe.wait_ge(hot_split, j + 1)
                pe.wait_ge(chunk_ready, T * chunks + (at + 1))
                for table in (hot_hi, hot_lo):
                    last = nc.tensor.matmul(ps, table[0:kh, j, c, :], onehot[0:kh, at % RING, :],
                                            start=(c == 0 and table is hot_hi), stop=(c == ROWS - 1 and table is hot_lo))
                last.then_inc(chunk_used, 1)

            def products(T, m):
                for done in (gram_act, gram_dve):
                    reach(pe, done, T * (HALVES * gram_half) + (m - 1))
                for g in range(per_fill):
                    b = ((m % gram_half) * per_fill + g) * QUAD
                    col = g * QUAD * feats
                    last = nc.tensor.matmul(gram_ps[m % 2][:, col:col + QUAD * feats],
                                            xt[:, b:b + QUAD, :].rearrange("p b f -> p (b f)"),
                                            xt[:, b:b + QUAD, 0:feats], start=True, stop=True)
                last.then_inc(gram_full, 1)

            def tail_has(kind, T, half):
                for b in range(2):
                    nth = [tail_nth[key] for key in tail if key[0] == kind and tail_bank[key] == b]
                    if nth:
                        pe.wait_ge(tail_copied[b], counted(T, half, tail_per[b], max(nth) + 1))

            def tail_step(T, key, part, half):
                kind, j = key
                bank = tail_bank[key]
                ps = tail_ps[bank]
                if part == 0:
                    if j == 0:
                        if kind == "cols":
                            for done in (gram_act, gram_dve):
                                pe.wait_ge(done, counted(T, half, gram_half, gram_half))
                        elif kind == "zt":
                            tail_has("cols", T, half)
                    reach(pe, tail_copied[bank], counted(T, half, tail_per[bank], tail_nth[key]))
                    if kind in ("cols", "zt"):
                        pe.sem_inc(stages_opened, 1)
                if kind == "cols":
                    for c, q in enumerate(col_groups[j]):
                        last = nc.tensor.transpose(ps[:, c * P:(c + 1) * P],
                                                   gram[:, q:q + 2, :].rearrange("p q g -> p (q g)"), ident[:, :])
                elif kind == "zt":
                    for n, (h, of) in enumerate(z_blocks[j]):
                        if n > 0:
                            last.then_inc(rest_turned, 1)
                            pe.wait_ge(rest_turned, counted(T, half, 1, 1))
                            pe.sem_inc(stages_opened, 1)
                        rows = slice(h * groups_half, (h + 1) * groups_half)
                        for s in range(QUAD):
                            last = nc.tensor.transpose(
                                ps[0:of.stop - of.start, s * groups_half:(s + 1) * groups_half],
                                z[rows, s, of], ident[rows, rows])
                elif kind in layer:
                    products_of = layer[kind]
                    w = slice(j * P, (j + 1) * P)
                    for n in range(2 * part, min(2 * part + 2, len(products_of))):
                        a, b, k = products_of[n]
                        if j == 0 and a == "hi":
                            if kind == "h1":
                                pe.wait_ge(zt_rounded if b == "hi" else zt_split, counted(T, half, n_kz, k + 1))
                            else:
                                pe.wait_ge(h1_rounded if b == "hi" else h1_split, counted(T, half, m1, k + 1))
                        if b == "x":
                            weights, moving = w1d_sb[:, w], dense_sb[:, bass.ds(counted(T, half, n_half, 0), n_half)]
                        elif kind == "h1":
                            weights = {"hi": w1z_hi, "lo": w1z_lo}[a][0:kz[k], k, w]
                            moving = {"hi": zt_hi, "lo": zt_lo}[b][0:kz[k], k, :]
                        else:
                            weights = {"hi": w2_hi, "lo": w2_lo}[a][:, k, w]
                            moving = {"hi": h1_hi, "lo": h1_lo}[b][:, k, :]
                        last = nc.tensor.matmul(ps[:, 0:n_half], weights, moving,
                                                start=(n == 0), stop=(n == len(products_of) - 1))
                else:
                    for c in range(m2):
                        h2_bank = tail_bank["h2", c]
                        pe.wait_ge(tail_copied[h2_bank], counted(T, half, tail_per[h2_bank], tail_nth["h2", c] + 1))
                        last = nc.tensor.matmul(ps[0:1, 0:n_half], w3_sb[:, c:c + 1], h2[:, c, :],
                                                start=(c == 0), stop=(c == m2 - 1))
                if part == parts[kind] - 1:
                    last.then_inc(tail_full[kind], 1)

            def walk(T, steps):
                for kind, *what in steps:
                    if kind == "ids":
                        hot_ids_spread(T + what[0] // (items // 2), what[0] % (items // 2))
                    elif kind == "chunk":
                        hot_chunk(T + what[0] // chunks, what[0] % chunks)
                    elif kind == "turn":
                        turn_rows(T, *what)
                    elif kind == "tail":
                        if isinstance(T, int) and T == 0 and what == [tail[0], 0, 1]:
                            pe.wait_ge(weights_in, 9 * 16)
                            pe.wait_ge(weights_split, len(weight_parts))
                        tail_step(T, *what)
                    elif kind == "gram":
                        half, first = divmod(what[0], gram_half)
                        if first % n_gram == 0:
                            k = half * tiles_half + first // n_gram
                            pe.wait_ge(x_copied, T * fills + (fill_no["turn", k, n_turn - 1] + 1))
                            pe.wait_ge(dense_copied, T * HALVES + (half + 1))
                        products(T, *what)

            pe.wait_ge(ident_ready, 1)
            pe.wait_ge(ids_row_ready, 2)
            walk(0, first_steps)
            pe.wait_ge(dense_in, 16)
            walk(0, plan(True, False))
            with pe.Fori(1, supers - 1) as T:
                walk(T, plan(False, False))
            walk(supers - 1, plan(False, True))
            for _, key, part in tail_steps:
                tail_step(supers, key, part, 0)

        @block.scalar
        def _(act):
            copy = nc.scalar.copy

            def hot_copy(T, at):
                T, at = T + at // chunks, at % chunks
                half, j = divmod(at // ROWS, nh)
                act.wait_ge(chunk_used, T * chunks + (at + 1))
                copy(xt[:, :, nf + j], x_ps[fill_no["hot", at // ROWS] % len(x_ps)][:, 0:n_half]).then_inc(x_copied, 1)
                if j == 0:
                    copy(xt[:, :, nf + nh], dense_sb[:, bass.ds(T * n_super + half * n_half, n_half)]
                         ).then_inc(dense_copied, 1)

            def walk(T, steps):
                waiting, grams = [], 0
                for kind, *what in steps:
                    if kind == "chunk":
                        at = what[0]
                        if at % ROWS == ROWS - 1:
                            if at // ROWS % nh < early // ROWS and at >= early:
                                waiting.append(at)
                            else:
                                hot_copy(T, at)
                    elif kind == "xt free":
                        for m, at in enumerate(waiting):
                            if m == 0:
                                act.wait_ge(gram_full, T * (HALVES * gram_half) + grams)
                            hot_copy(T, at)
                        waiting = []
                    elif kind == "turn":
                        k, g = what
                        fs = turn_groups[g]
                        act.wait_ge(turn_full[k], T * n_turn + (g + 1))
                        n = fill_no["turn", k, g]
                        b = (k % tiles_half) * P
                        src = x_ps[n % len(x_ps)][:, 0:len(fs) * P].rearrange("p (f b) -> p b f", b=P)
                        copy(xt[:, b:b + P, fs[0]:fs[-1] + 1], src).then_inc(x_copied, 1)
                    elif kind == "tail":
                        key, part, half = what
                        if part == parts[key[0]] - 1:
                            tail_copy(act, T, half, key)
                    elif kind == "gram":
                        gram_copy(act, copy, gram_act, (0, 1), T, *what)
                        grams = what[0] + 1

            for j in range(nh):
                act.wait_ge(hot_landed[j], 16)
                copy(hot_hi[0:kh, j, :, :].rearrange("p c d -> p (c d)"), hot_in[j]).then_inc(hot_rounded, 1)
            act.wait_ge(xt_cleared, 1)
            act.wait_ge(dense_in, 16)
            walk(0, first_steps)
            act.wait_ge(weights_in, 9 * 16)
            for hi, _, src in weight_parts:
                copy(hi, src).then_inc(weights_rounded, 1)
            walk(0, plan(True, False))
            with act.Fori(1, supers - 1) as T:
                walk(T, plan(False, False))
            walk(supers - 1, plan(False, True))
            for key in tail:
                tail_copy(act, supers, 0, key)
            act.wait_ge(tail_copied[tail_bank["y", 0]], supers * HALVES * tail_per[tail_bank["y", 0]])
            act.dma_start(out, dense_sb[0:1, :]).then_inc(y_stored, 16)
            act.wait_ge(y_stored, 16)

        @block.vector
        def _(dve):
            copy = nc.vector.tensor_copy

            def make_chunk(T, at):
                item, c = divmod(at, ROWS)
                if isinstance(T, int) and T == 0 and item < nh and c == 0:
                    dve.wait_ge(hot_rounded, item + 1)
                    nc.vector.tensor_tensor(hot_lo[0:kh, item, :, :].rearrange("p c d -> p (c d)"), hot_in[item],
                                            hot_hi[0:kh, item, :, :].rearrange("p c d -> p (c d)").bitcast(F32),
                                            ALU.subtract).then_inc(hot_split, 1)
                if at % (2 * ROWS) == 0:
                    dve.wait_ge(ids_full, T * (items // 2) + (item // 2 + 1))
                reach(dve, chunk_used, T * chunks + (at + 1 - RING))
                nc.vector.tensor_scalar(onehot[0:kh, at % RING, :], ids_ps[0:kh, item % 2, :],
                                        row_no[0:kh, c:c + 1], None, ALU.is_equal).then_inc(chunk_ready, 1)

            def walk(T, steps):
                for kind, *what in steps:
                    if kind == "chunk":
                        for at in made_at(what[0]):
                            if at < chunks or not (isinstance(T, int) and T == supers - 1):
                                make_chunk(T + at // chunks, at % chunks)
                    elif kind == "tail":
                        key, part, half = what
                        if part == parts[key[0]] - 1:
                            tail_split(dve, T, half, key)
                    elif kind == "gram":
                        if isinstance(T, int) and T == 0 and what[0] in split_at:
                            n = split_at.index(what[0])
                            hi, lo, src = weight_parts[n]
                            dve.wait_ge(weights_rounded, n + 1)
                            nc.vector.tensor_tensor(lo, src, hi.bitcast(F32), ALU.subtract).then_inc(weights_split, 1)
                        gram_copy(dve, copy, gram_dve, (2, 3), T, *what)

            split_at = [2, 4, 6, 8, 10]
            dve.wait_ge(ids_row_landed, 16)
            copy(ids_row[:, :], ids_row_in).then_inc(ids_row_ready, 1)
            dve.wait_ge(ids_row_ready, 1)
            dve.wait_ge(consts_ready, 4)
            copy(pick[:, :, :].rearrange("j k p -> j (k p)"), pick_in).then_inc(ids_row_ready, 1)
            for at in range(LEAD):
                make_chunk(0, at)
            nc.vector.memset(xt[:, :, feats:], 0.0).then_inc(xt_cleared, 1)
            walk(0, first_steps)
            walk(0, plan(True, False))
            with dve.Fori(1, supers - 1) as T:
                walk(T, plan(False, False))
            walk(supers - 1, plan(False, True))
            for key in tail:
                if key[0] == "cols":
                    dve.wait_ge(tail_full["cols"], supers * HALVES * n_cols - n_cols + key[1] + 1)
                    pairs_copy(copy, key[1], 1).then_inc(odd_copied, 1)
                tail_split(dve, supers, 0, key)


def kernel(**inputs):
    import numpy as np
    import concourse.bacc as bacc
    from concourse.bass_utils import run_bass_kernel_spmd

    batch, n_tables = inputs["ids"].shape
    rows = [inputs[f"tbl_{f}"].shape[0] for f in range(n_tables)]
    hot = sorted(range(n_tables), key=lambda f: rows[f])[:HOT]
    cold = [f for f in range(n_tables) if f not in hot]
    order = cold + hot + [n_tables]
    start = [i * (n_tables + 1) - i * (i + 1) // 2 for i in range(n_tables + 1)]
    halves = [[start[min(a, b)] + abs(a - b) - 1 for n, a in list(enumerate(order))[h:-1:2] for b in order[n + 1:]]
              for h in range(2)]
    rest = len(halves[0]) - 64
    pair_rows = halves[0][:rest] + halves[1][:P] + halves[0][rest:] + halves[1][P:]
    w1 = np.asarray(inputs["W_top1"])
    ids = np.asarray(inputs["ids"])
    arrays = {
        "dense_t": inputs["r_dense_x"].T,
        "ids": ids[:, cold].reshape(batch // P, P, len(cold)).transpose(1, 0, 2),
        "hot_ids": ids[:, hot].T,
        "w1": np.concatenate([w1[pair_rows], w1[len(pair_rows):]]),
        "b1": np.asarray(inputs["b_top1"]).reshape(-1, P).T,
        "w2": inputs["W_top2"],
        "b2": np.asarray(inputs["b_top2"]).reshape(-1, P).T,
        "w3": np.asarray(inputs["W_top3"]).reshape(-1, P).T,
    }
    for f in range(n_tables):
        arrays[f"tbl_{f}"] = inputs[f"tbl_{f}"]
    arrays = {n: np.ascontiguousarray(a) for n, a in arrays.items()}
    nc = bacc.Bacc("TRN2", target_bir_lowering=False, num_devices=1)
    ap = {n: nc.dram_tensor(f"in_{n}", a.shape, mybir.dt.from_np(a.dtype), kind="ExternalInput").ap()
          for n, a in arrays.items()}
    y = nc.dram_tensor("y_out", (1, batch), F32, kind="ExternalOutput").ap()
    build(nc, ap["dense_t"], ap["ids"], ap["hot_ids"], [ap[f"tbl_{f}"] for f in cold], [ap[f"tbl_{f}"] for f in hot],
          ap["w1"], ap["b1"], ap["w2"], ap["b2"], ap["w3"], y)
    r = run_bass_kernel_spmd(nc, [{f"in_{n}": a for n, a in arrays.items()}], core_ids=[0])
    return r.results[0]["y_out"].reshape(batch, 1)
```
